# Optimizing a Trainium2 kernel written in Bass

```python
import numpy as np
import jax
import jax.numpy as jnp

def _softmax(x, axis=-1):
    return jax.nn.softmax(x, axis=axis)

def _gelu(x):
    return jax.nn.gelu(x, approximate=True)

def _silu(x):
    return jax.nn.silu(x)

def _sigmoid(x):
    return jax.nn.sigmoid(x)

def _layernorm(x, axis=-1, eps=1e-05):
    m = jnp.mean(x, axis=axis, keepdims=True)
    v = jnp.var(x, axis=axis, keepdims=True)
    return (x - m) / jnp.sqrt(v + eps)

def _scatter_add(tgt, idx, src, axis=0):
    return tgt.at[idx].add(src)

def _segment_sum(src, seg, n):
    return jax.ops.segment_sum(src, seg, n)
kernel_name = 'mk_adj_resnorm_d1_adj_r2_2981d6'

def setup_inputs(seed: int=0):
    np.random.seed(seed)
    _w = jnp.asarray

    def _rec_inputs():
        import jax
        import jax.numpy as jnp
        _gk = jax.random.key(seed)
        x = -0.000929 + 1 * jax.random.normal(jax.random.fold_in(_gk, 1), (8192, 64), jnp.float32)
        _w = (1.0 + jnp.arange(8192, dtype=jnp.float32)) ** (-0.5)
        _w = _w / _w.mean()
        _pij = jnp.clip(0.00195312 * _w[:, None] * _w[None, :], 0.0, 1.0)
        _a = jax.random.uniform(jax.random.fold_in(_gk, 2), (8192, 8192)) < _pij
        _a = jnp.logical_or(_a, jnp.eye(8192, dtype=bool))
        _af = _a.astype(jnp.float32)
        _af = _af * jax.random.uniform(jax.random.fold_in(_gk, 3), (8192, 8192), jnp.float32, 0.05, 1)
        adj = _af
        return (x, adj)
    x, adj = _rec_inputs()

    def _L0_gnn_setup():
        import jax, jax.numpy as jnp
        import numpy as np
        N = 8192
        F_IN = 64
        F_OUT = 64
        key = jax.random.key(seed)
        k1, k2, k3 = jax.random.split(key, 3)
        inp = jax.random.normal(k1, (N, F_IN), dtype=jnp.float32)
        adj = jax.random.uniform(k2, (N, N), dtype=jnp.float32)
        limit = np.sqrt(6.0 / (F_IN + F_OUT)).astype(np.float32)
        W = jax.random.uniform(k3, (F_IN, F_OUT), dtype=jnp.float32, minval=-limit, maxval=limit)
        b = jnp.zeros((F_OUT,), dtype=jnp.float32)
        return {'input': inp, 'adj': adj, 'W': W, 'b': b}
    _L0_gnn_all = _L0_gnn_setup()
    _L0_gnn_in = {k: v for k, v in _L0_gnn_all.items() if k in ('W', 'b')}
    del _L0_gnn_all
    return {'x': x, 'adj': adj, 'L0_gnn_W': _L0_gnn_in['W'], 'L0_gnn_b': _L0_gnn_in['b']}

def reference(x, adj, L0_gnn_W, L0_gnn_b):
    import jax
    import jax.numpy as jnp

    def _L0_gnn_ref(input, adj, W, b):
        import jax, jax.numpy as jnp
        import numpy as np
        N = 8192
        F_IN = 64
        F_OUT = 64
        h = input @ W
        out = adj @ h + b
        return out
    x = _layernorm(x + _L0_gnn_ref(x, adj, L0_gnn_W, L0_gnn_b), axis=-1)
    return x

_drawn_inputs = setup_inputs


def setup_inputs(seed=0):
    import zlib

    import numpy as np

    out = dict(_drawn_inputs(seed))
    spreads = {'L0_gnn_b': (0.0, 0.1)}
    factors = {}
    for name, (base, spread) in spreads.items():
        noise = np.random.default_rng([zlib.crc32(name.encode()), seed]).standard_normal(out[name].shape)
        drawn = base * np.exp(spread * noise) if base else spread * noise
        out[name] = jnp.asarray(drawn.astype(out[name].dtype))
    for name, factor in factors.items():
        out[name] = (out[name] * factor).astype(out[name].dtype)
    return out
```

```python
import concourse.bass as bass
from concourse import mybir
from contextlib import ExitStack


def gnn_residual_layernorm(nc: bass.Bass, x: bass.AP, adj: bass.AP, w: bass.AP, bias: bass.AP, out: bass.AP):
    fp32 = mybir.dt.float32
    ALU = mybir.AluOpType
    ACT = mybir.ActivationFunctionType
    ENG = mybir.EngineType

    P = 128
    SQ = 32
    NQ = P // SQ
    N, F = x.shape
    QUAD = N // NQ
    CHUNKS = QUAD // SQ
    ROWS = 512
    BLOCKS = N // ROWS
    SUB = ROWS // SQ
    TILES = ROWS // P
    WIDTH = 512
    PIECES = QUAD // WIDTH
    CPP = WIDTH // SQ
    HC = CPP // 2
    UNITS = 2 * PIECES
    US = SUB // 2
    RAW = 4
    TRN = 2
    PARTS = 4
    PC = CPP // PARTS
    LOTS = {k: [(part, 0, SUB) for part in range(PARTS)] for k in range(1, PIECES)}
    LOTS[PIECES - 1][-1:] = [(PARTS - 1, 0, US), (PARTS - 1, US, SUB)]
    XP = N // P
    XB = ROWS // XP
    BPQ = BLOCKS // NQ
    GROUP = 4
    GROUPS = SQ // GROUP
    EPS = 1e-5
    assert UNITS % RAW == 0 and PIECES % TRN == 0 and XP == 2 * SQ and CHUNKS == XP

    ctx = ExitStack()
    with ctx:
        def sb(name, shape):
            return ctx.enter_context(nc.sbuf_tensor(name, shape, fp32))

        def pb(name, shape):
            return ctx.enter_context(nc.psum_tensor(name, shape, fp32))

        def sem(name):
            return ctx.enter_context(nc.semaphore(name))

        raw = sb("raw", [P, RAW, US * WIDTH])
        trn = sb("trn", [P, TRN, CPP, SUB, SQ])
        h = sb("h", [P, CHUNKS, F])
        x_sb = trn[:, TRN - 1, HC:CPP, :, :].rearrange("p c s q -> p (c s q)").rearrange(
            "p (m k) -> p m k", k=F)
        x_t = sb("x_t", [P, SQ, NQ, SQ])
        w2 = sb("w2", [P, 2, F])
        bias_col = sb("bias_col", [P, 1])
        ident = sb("ident", [P, P])
        fold = sb("fold", [P, F])
        sum_t = sb("sum_t", [P, 2, ROWS])
        y = sb("y", [P, TILES, F])
        centred = sb("centred", [P, TILES, F])
        normed = sb("normed", [P, 2, TILES, F])
        stats = sb("stats", [P, TILES, 6])
        moments = sb("moments", [P, TILES, 2])
        var_eps = sb("var_eps", [P, TILES])
        rstd = sb("rstd", [P, TILES])
        eps = sb("eps", [P, TILES])
        minus_half = sb("minus_half", [P, TILES])

        acc = [pb(f"acc{i}", [P, ROWS]) for i in range(2)]
        rows_ps = pb("rows_ps", [P, TILES, F])
        xt_ps = acc
        h_ps = [pb(f"h_ps{g}", [P, GROUP * 2 * F]) for g in range(2)]

        x_landed = sem("x_landed")
        w_landed = sem("w_landed")
        rest_zeroed = sem("rest_zeroed")
        bias_landed = sem("bias_landed")
        unit_landed = [sem(f"unit_landed{i}") for i in range(RAW)]
        lot_landed = {k: [sem(f"lot_landed{k}_{i}") for i in range(len(LOTS[k]))] for k in LOTS}
        consts_zeroed = sem("consts_zeroed")
        consts_ready = sem("consts_ready")
        x_transposed = sem("x_transposed")
        x_t_ready = sem("x_t_ready")
        h_done = sem("h_done")
        h_ready = sem("h_ready")
        half_ready = sem("half_ready")
        half_used = sem("half_used")
        sum_left = sem("sum_left")
        sum_ready = sem("sum_ready")
        rows_ready = sem("rows_ready")
        y_ready = sem("y_ready")
        moments_ready = sem("moments_ready")
        var_eps_ready = sem("var_eps_ready")
        rstd_ready = sem("rstd_ready")
        centred_ready = sem("centred_ready")
        normed_ready = sem("normed_ready")
        last_stored = sem("last_stored")
        stored = [sem(f"stored{i}") for i in range(2)]

        adj_v = adj.rearrange("(b g s q) (a k w) -> b a k g q s w", g=2, s=US, q=SQ, a=NQ, k=PIECES)
        adj_parts = adj.rearrange("(b s q) (a j w) -> b a j q s w", s=SUB, q=SQ, a=NQ, w=PC * SQ)
        out_v = out.rearrange("(b p t) k -> b p t k", b=BLOCKS, t=TILES)
        x_t_blocks = x_t[:, :, :, :].rearrange("k (b v) a r -> k b a v r", b=BPQ)
        LAST = BLOCKS - 1

        block = ctx.enter_context(nc.Block())

        def over_blocks(engine, body):
            for b in (0, 1):
                body(b, b, True)
            with nc.Fori(1, BLOCKS // 2 - 1, 1, engines=[engine]) as i:
                for parity in range(2):
                    body(i * 2 + parity, parity, False)
            for b in (LAST - 1, LAST):
                body(b, b % 2, False)

        def in_parts(b, k):
            return isinstance(b, int) and b == LAST and k in LOTS


        def load_unit(eng, b, u, quadrants):
            if not (isinstance(b, int) and b == 0 and u < RAW):
                eng.wait_ge(half_ready, (b * UNITS + u - RAW + 1) * 2)
            for a in quadrants:
                at = slice(a * SQ, (a + 1) * SQ)
                if not in_parts(b, u // 2):
                    eng.dma_start(raw[at, u % RAW, :].rearrange("q (s w) -> q s w", w=WIDTH),
                                  adj_v[b, a, u // 2, u % 2]).then_inc(unit_landed[u % RAW], 16)
            if in_parts(b, u // 2):
                k = u // 2
                for n, (part, s0, s1) in enumerate(LOTS[k]):
                    if part // 2 == u % 2:
                        for a in quadrants:
                            eng.dma_start(part_slot(k, part)[a * SQ:(a + 1) * SQ, s0:s1],
                                          adj_parts[b, a, k * PARTS + part][:, s0:s1]
                                          ).then_inc(lot_landed[k][n], 16)

        def part_slot(k, part):
            u = 2 * k + part // 2
            half = US * WIDTH // 2
            return raw[:, u % RAW, (part % 2) * half:(part % 2 + 1) * half].rearrange(
                "p (s w) -> p s w", s=SUB)

        @block.sync
        def _(sp):
            sp.dma_start(x_sb, x.rearrange("(p m) k -> p m k", m=XP)).then_inc(x_landed, 16)

            def body(b, parity, peeled):
                for u in range(UNITS):
                    load_unit(sp, b, u, (0, 1))

            over_blocks(ENG.SP, body)
            sp.wait_ge(normed_ready, BLOCKS)
            sp.dma_start(out_v[LAST], normed[:, LAST % 2, :, :]).then_inc(last_stored, 16)
            sp.wait_ge(stored[0], BLOCKS // 2 * 16)
            sp.wait_ge(stored[1], (BLOCKS // 2 - 1) * 16)
            sp.wait_ge(last_stored, 16)

        @block.scalar
        def _(act):
            act.wait_ge(rest_zeroed, 2)
            for e in range(2):
                act.dma_start(w2[e * F:(e + 1) * F, e, :], w).then_inc(w_landed, 16)
            act.dma_start(bias_col[0:F, :], bias.rearrange("(f a) -> f a", a=1)).then_inc(bias_landed, 16)
            for u in range(RAW):
                load_unit(act, 0, u, (2, 3))
            for g in range(GROUPS):
                act.wait_ge(x_transposed, g + 1)
                for a in range(NQ):
                    last = nc.scalar.copy(
                        x_t[:, :, a, g * GROUP:(g + 1) * GROUP],
                        xt_ps[g % 2][:, :].rearrange("k (r a v) -> k a v r", r=GROUP, a=NQ)[:, a])
                last.then_inc(x_t_ready, 1)
            for g in range(GROUPS):
                act.wait_ge(h_done, g + 1)
                nc.scalar.copy(h[:, g * 2 * GROUP:(g + 1) * 2 * GROUP, :].rearrange("p c f -> p (c f)"),
                               h_ps[g % 2][:, :]).then_inc(h_ready, 1)
            act.wait_ge(bias_landed, 16)

            def evacuate(b, parity):
                act.wait_ge(half_used, (b + 1) * PIECES * 2)
                nc.scalar.activation(sum_t[:, parity, :], acc[parity][:, :], ACT.Identity,
                                     bias=bias_col[:, 0:1]).then_inc(sum_left, 1)

            def body(b, parity, peeled):
                for u in range(UNITS):
                    if not (peeled and parity == 0 and u < RAW):
                        load_unit(act, b, u, (2, 3))
                    if u == 6 and not (peeled and parity == 0):
                        evacuate(b - 1, 1 - parity)

            over_blocks(ENG.Activation, body)
            evacuate(LAST, LAST % 2)

        @block.tensor
        def _(pe):
            pe.wait_ge(consts_ready, 1)
            pe.wait_ge(x_landed, 16)
            for g in range(GROUPS):
                if g >= 2:
                    pe.wait_ge(x_t_ready, g - 1)
                for n in range(GROUP):
                    for e in range(2):
                        last = nc.tensor.matmul(xt_ps[g % 2][e * F:(e + 1) * F, n * P:(n + 1) * P],
                                                x_sb[:, e * SQ + g * GROUP + n, :], ident[:, :],
                                                start=True, stop=True)
                last.then_inc(x_transposed, 1)
            pe.wait_ge(w_landed, 32)
            pe.wait_ge(x_t_ready, GROUPS)
            for g in range(GROUPS):
                if g >= 2:
                    pe.wait_ge(h_ready, g - 1)
                for n in range(GROUP):
                    last = nc.tensor.matmul(
                        h_ps[g % 2][:, n * 2 * F:(n + 1) * 2 * F],
                        x_t[:, g * GROUP + n, :, :].rearrange("k a r -> k (a r)"),
                        w2[:, :, :].rearrange("k e f -> k (e f)"), start=True, stop=True)
                last.then_inc(h_done, 1)
            pe.wait_ge(h_ready, GROUPS)

            def multiply(b, parity, k, chunks):
                for c in chunks:
                    chunk = k * CPP + c
                    e = chunk % 2
                    last = nc.tensor.matmul(acc[parity][e * F:(e + 1) * F, :], h[:, chunk, :],
                                            trn[:, k % TRN, c, :, :].rearrange("p s q -> p (s q)"),
                                            start=(chunk < 2), stop=(chunk >= CHUNKS - 2))
                return last

            def to_rows(b, parity, zeroth):
                pe.wait_ge(sum_ready, b + 1)
                if not zeroth:
                    pe.wait_ge(y_ready, b)
                for t in range(TILES):
                    last = nc.tensor.matmul(rows_ps[:, t, :],
                                            sum_t[:, parity, :].rearrange("m (p t) -> m t p", t=TILES)[:, t, :],
                                            fold[:, :], start=True, stop=True)
                last.then_inc(rows_ready, 1)

            def body(b, parity, peeled):
                first = peeled and parity == 0
                if not peeled:
                    pe.wait_ge(sum_left, b - 1)
                for k in range(PIECES):
                    if in_parts(b, k):
                        for part in range(PARTS):
                            lots = sum(p <= part for p, _, _ in LOTS[k])
                            pe.wait_ge(half_ready, (b * UNITS + 2 * k) * 2 + lots)
                            last = multiply(b, parity, k, range(part * PC, (part + 1) * PC))
                            if part % 2:
                                last.then_inc(half_used, 1)
                    else:
                        for half in range(2):
                            pe.wait_ge(half_ready, (b * UNITS + 2 * k + 1) * 2 + half + 1)
                            multiply(b, parity, k, range(half * HC, (half + 1) * HC)).then_inc(half_used, 1)
                    if k == 1 and not first:
                        to_rows(b - 1, 1 - parity, peeled)

            over_blocks(ENG.PE, body)
            to_rows(LAST, LAST % 2, False)

        def centre(eng, b):
            eng.tensor_tensor(centred[:, :, :], y[:, :, :], moments[:, :, 0:1].to_broadcast([P, TILES, F]),
                              ALU.subtract).then_inc(centred_ready, 1)

        def scale(eng, b, parity):
            eng.wait_ge(centred_ready, b + 1)
            eng.wait_ge(rstd_ready, b + 1)
            eng.tensor_tensor(normed[:, parity, :, :], centred[:, :, :],
                              rstd[:, :].rearrange("p (t a) -> p t a", a=1).to_broadcast([P, TILES, F]),
                              ALU.mult).then_inc(normed_ready, 1)

        @block.vector
        def _(dve):
            def add_x(b, parity):
                dve.wait_ge(sum_left, b + 1)
                for e in range(2):
                    at = slice(e * F, (e + 1) * F)
                    part = sum_t[at, parity, :].rearrange("k (v e r) -> k e v r", e=2, r=SQ)[:, e]
                    last = nc.vector.tensor_tensor(part, part, x_t_blocks[at, b % BPQ, b // BPQ], ALU.add)
                last.then_inc(sum_ready, 1)

            def row_stats(b, zeroth):
                if not zeroth:
                    dve.wait_ge(centred_ready, b)
                dve.wait_ge(rows_ready, b + 1)
                for t in range(TILES):
                    nc.vector.bn_stats(stats[:, t, :], rows_ps[:, t, :])
                nc.vector.tensor_copy(y[:, :, :], rows_ps[:, :, :]).then_inc(y_ready, 1)

            def row_moments(b):
                dve.drain()
                for t in range(TILES):
                    last = nc.vector.bn_aggr(moments[:, t, :], stats[:, t, :])
                last.then_inc(moments_ready, 1)

            def body(b, parity, peeled):
                first = peeled and parity == 0
                for u in range(UNITS):
                    k, g = u // 2, u % 2
                    if in_parts(b, k):
                        for n, (part, s0, s1) in enumerate(LOTS[k]):
                            if part // 2 != g:
                                continue
                            dve.wait_ge(lot_landed[k][n], 16 * NQ)
                            if part % 2 == 0:
                                dve.wait_ge(half_used, (b * PIECES + k - TRN) * 2 + g + 1)
                            nc.vector.transpose(
                                trn[:, k % TRN, part * PC:(part + 1) * PC, s0:s1, :],
                                part_slot(k, part)[:, s0:s1].rearrange("p s (c r) -> p c s r", r=SQ),
                            ).then_inc(half_ready, 1)
                    else:
                        dve.wait_ge(unit_landed[u % RAW], (b * (UNITS // RAW) + u // RAW + 1) * 16 * NQ)
                        for half in range(2):
                            if g == 0:
                                if not (first and k < TRN):
                                    dve.wait_ge(half_used, (b * PIECES + k - TRN) * 2 + half + 1)
                                elif k == TRN - 1 and half == 1:
                                    dve.wait_ge(x_transposed, GROUPS)
                            c = half * HC
                            nc.vector.transpose(
                                trn[:, k % TRN, c:c + HC, g * US:(g + 1) * US, :],
                                raw[:, u % RAW, :].rearrange("p (s c r) -> p c s r", s=US, r=SQ)[:, c:c + HC],
                            ).then_inc(half_ready, 1)
                    if not first:
                        if u == 3:
                            add_x(b - 1, 1 - parity)
                        elif u == 5:
                            row_stats(b - 1, peeled)
                        elif u == 6:
                            row_moments(b - 1)

            over_blocks(ENG.DVE, body)
            add_x(LAST, LAST % 2)
            row_stats(LAST, False)
            row_moments(LAST)
            dve.wait_ge(normed_ready, LAST)
            dve.wait_ge(moments_ready, BLOCKS)
            centre(dve, LAST)
            dve.wait_ge(stored[LAST % 2], (LAST // 2) * 16)
            scale(dve, LAST, LAST % 2)

        @block.gpsimd
        def _(pool):
            pool.memset(w2[:, :, :], 0.0).then_inc(rest_zeroed, 1)
            pool.memset(bias_col[:, :], 0.0).then_inc(rest_zeroed, 1)
            pool.memset(ident[:, :], 0.0).then_inc(consts_zeroed, 1)
            pool.memset(fold[:, :], 0.0).then_inc(consts_zeroed, 1)
            pool.memset(minus_half[:, :], -0.5).then_inc(consts_zeroed, 1)
            pool.memset(eps[:, :], EPS).then_inc(consts_zeroed, 1)
            pool.wait_ge(consts_zeroed, 4)
            pool.affine_select(out=ident[:, :], in_=ident[:, :], compare_op=ALU.not_equal, fill=1.0,
                               base=0, pattern=[[-1, P]], channel_multiplier=1).then_inc(consts_zeroed, 1)
            pool.affine_select(out=fold[:, :], in_=fold[:, :], compare_op=ALU.not_equal, fill=1.0,
                               base=0, pattern=[[-1, F]], channel_multiplier=1).then_inc(consts_zeroed, 1)
            pool.wait_ge(consts_zeroed, 6)
            pool.affine_select(out=fold[:, :], in_=fold[:, :], compare_op=ALU.not_equal, fill=1.0,
                               base=-F, pattern=[[-1, F]], channel_multiplier=1).then_inc(consts_ready, 1)

            def deviation(b):
                pool.wait_ge(moments_ready, b + 1)
                pool.tensor_tensor(var_eps[:, :], moments[:, :, 1], eps[:, :], ALU.add).then_inc(var_eps_ready, 1)
                pool.wait_ge(var_eps_ready, b + 1)
                pool.tensor_tensor(rstd[:, :], var_eps[:, :], minus_half[:, :], ALU.pow).then_inc(rstd_ready, 1)

            def normalise(b, parity, first):
                deviation(b)
                centre(pool, b)
                if not first:
                    pool.wait_ge(stored[parity], (b // 2) * 16)
                scale(pool, b, parity)
                pool.wait_ge(normed_ready, b + 1)
                pool.dma_start(out_v[b], normed[:, parity, :, :]).then_inc(stored[parity], 16)

            for b in (0, 1):
                normalise(b, b, True)
            with nc.Fori(1, BLOCKS // 2 - 1, 1, engines=[ENG.Pool]) as i:
                for parity in range(2):
                    normalise(i * 2 + parity, parity, False)
            normalise(LAST - 1, (LAST - 1) % 2, False)
            deviation(LAST)


_INS = ['x', 'adj', 'L0_gnn_W', 'L0_gnn_b']
_OUTS = [((8192, 64), 'float32')]


def kernel(**inputs):
    import numpy as _np
    import concourse.bacc as _bacc
    from concourse import mybir as _mybir
    from concourse.bass_utils import run_bass_kernel_spmd as _run

    nc = _bacc.Bacc("TRN2", target_bir_lowering=False, num_devices=1)
    arrays, args = {}, []
    for name in _INS:
        a = _np.ascontiguousarray(inputs[name])
        arrays[f"in_{name}_dram"] = a
        args.append(nc.dram_tensor(f"in_{name}_dram", a.shape, _mybir.dt.from_np(a.dtype), kind="ExternalInput").ap())
    for i, (shape, dtype) in enumerate(_OUTS):
        dt = _mybir.dt.from_np(_np.dtype(dtype))
        args.append(nc.dram_tensor(f"out_{i}_dram", shape, dt, kind="ExternalOutput").ap())
    gnn_residual_layernorm(nc, *args)
    r = _run(nc, [arrays], core_ids=[0])
    return r.results[0]["out_0_dram"]
```
